# Optimizing a Trainium2 kernel written in Bass

```python
import numpy as np
import jax
import jax.numpy as jnp

def _softmax(x, axis=-1):
    return jax.nn.softmax(x, axis=axis)

def _gelu(x):
    return jax.nn.gelu(x, approximate=True)

def _silu(x):
    return jax.nn.silu(x)

def _sigmoid(x):
    return jax.nn.sigmoid(x)

def _layernorm(x, axis=-1, eps=1e-05):
    m = jnp.mean(x, axis=axis, keepdims=True)
    v = jnp.var(x, axis=axis, keepdims=True)
    return (x - m) / jnp.sqrt(v + eps)

def _scatter_add(tgt, idx, src, axis=0):
    return tgt.at[idx].add(src)

def _segment_sum(src, seg, n):
    return jax.ops.segment_sum(src, seg, n)
kernel_name = 'mk_cond_resid_d4_seqx_r8_9076ea'

def setup_inputs(seed: int=0):
    np.random.seed(seed)
    _w = jnp.asarray

    def _rec_inputs():
        import jax
        import jax.numpy as jnp
        _rk = jax.random.key(seed)
        x = -0.000125 + 0.9999 * jax.random.normal(jax.random.fold_in(_rk, 1), (16, 128, 128), jnp.float32)
        _lenS = 128 - jax.random.randint(jax.random.fold_in(_rk, 7), (16,), 0, max(1, 128 // 4) + 1, jnp.int32)
        _lenS2 = 128 - jax.random.randint(jax.random.fold_in(_rk, 8), (16,), 0, max(1, 128 // 4) + 1, jnp.int32)
        cond_8 = jax.random.uniform(jax.random.fold_in(_rk, 11), (16, 8), jnp.float32, 0.0, 0.983423)
        return (x, cond_8)
    x, cond_8 = _rec_inputs()

    def _L0_cond_setup():
        import jax, jax.numpy as jnp
        import numpy as np
        B, S, D = (16, 256, 128)
        E, H = (8, 256)
        key = jax.random.key(seed)
        ks = jax.random.split(key, 8)
        scale = 0.02
        x = jax.random.normal(ks[0], (B, S, D), dtype=jnp.float32)
        opcode_onehot = jax.random.uniform(ks[1], (B, E), dtype=jnp.float32)
        W_up = jax.random.normal(ks[2], (E, H, D), dtype=jnp.float32) * scale
        b_up = jnp.zeros((E, H), dtype=jnp.float32)
        W_gate = jax.random.normal(ks[3], (E, H, D), dtype=jnp.float32) * scale
        b_gate = jnp.zeros((E, H), dtype=jnp.float32)
        W_down = jax.random.normal(ks[4], (E, D, H), dtype=jnp.float32) * scale
        b_down = jnp.zeros((E, D), dtype=jnp.float32)
        return {'x': x, 'opcode_onehot': opcode_onehot, 'W_up': W_up, 'b_up': b_up, 'W_gate': W_gate, 'b_gate': b_gate, 'W_down': W_down, 'b_down': b_down}
    _L0_cond_all = _L0_cond_setup()
    _L0_cond_in = {k: v for k, v in _L0_cond_all.items() if k in ('W_up', 'b_up', 'W_gate', 'b_gate', 'W_down', 'b_down')}
    del _L0_cond_all

    def _L1_cond_setup():
        import jax, jax.numpy as jnp
        import numpy as np
        R = 16
        ALPHA = 32.0
        SCALING = ALPHA / R
        key = jax.random.key(seed)
        ks = jax.random.split(key, 6)
        B, T, C, O, E = (16, 1500, 128, 128, 8)
        x = jax.random.normal(ks[0], (B, T, C), dtype=jnp.float32)
        w = jax.random.uniform(ks[1], (B, E), dtype=jnp.float32)
        W_base = jax.random.normal(ks[2], (O, C), dtype=jnp.float32) * 0.02
        b_base = jax.random.normal(ks[3], (O,), dtype=jnp.float32) * 0.02
        As = jax.random.normal(ks[4], (E, R, C), dtype=jnp.float32) * 0.02
        Bs = jax.random.normal(ks[5], (E, O, R), dtype=jnp.float32) * 0.02
        return {'x': x, 'w': w, 'W_base': W_base, 'b_base': b_base, 'As': As, 'Bs': Bs}
    _L1_cond_all = _L1_cond_setup()
    _L1_cond_in = {k: v for k, v in _L1_cond_all.items() if k in ('W_base', 'b_base', 'As', 'Bs')}
    del _L1_cond_all

    def _L2_cond_setup():
        import jax, jax.numpy as jnp
        import numpy as np
        key = jax.random.key(seed)
        k1, k2, k3, k4, k5 = jax.random.split(key, 5)
        B, N, T, O, G = (32, 32, 128, 128, 8)
        x = jax.random.normal(k1, (B, N, T), dtype=jnp.float32)
        y = jax.random.uniform(k2, (B, G), dtype=jnp.float32)
        weight = jax.random.normal(k3, (G, O, T), dtype=jnp.float32) * (1.0 / np.sqrt(T))
        mask = jax.random.uniform(k4, (O, T), dtype=jnp.float32)
        bias = jax.random.normal(k5, (O,), dtype=jnp.float32)
        return {'x': x, 'y': y, 'weight': weight, 'mask': mask, 'bias': bias}
    _L2_cond_all = _L2_cond_setup()
    _L2_cond_in = {k: v for k, v in _L2_cond_all.items() if k in ('weight', 'mask', 'bias')}
    del _L2_cond_all

    def _L3_cond_setup():
        import jax, jax.numpy as jnp
        import numpy as np
        TOP_K = 2
        NUM_MOE_LAYERS = 12

        def _gemma_mlp(x, gate_w, up_w, down_w):
            g = jnp.einsum('bsh,hi->bsi', x, gate_w)
            u = jnp.einsum('bsh,hi->bsi', x, up_w)
            return jnp.einsum('bsi,ih->bsh', jax.nn.gelu(g, approximate=True) * u, down_w)
        key = jax.random.key(seed)
        ks = jax.random.split(key, 8)
        B, S, H, I, E = (32, 32, 128, 512, 8)
        std = 0.02
        return {'x': jax.random.normal(ks[0], (B, S, H), jnp.float32), 'router_logits': jax.random.normal(ks[1], (B, E), jnp.float32), 'skill_gate': jax.random.normal(ks[2], (E, H, I), jnp.float32) * std, 'skill_up': jax.random.normal(ks[3], (E, H, I), jnp.float32) * std, 'skill_down': jax.random.normal(ks[4], (E, I, H), jnp.float32) * std, 'shared_gate': jax.random.normal(ks[5], (H, I), jnp.float32) * std, 'shared_up': jax.random.normal(ks[6], (H, I), jnp.float32) * std, 'shared_down': jax.random.normal(ks[7], (I, H), jnp.float32) * std}
    _L3_cond_all = _L3_cond_setup()
    _L3_cond_in = {k: v for k, v in _L3_cond_all.items() if k in ('skill_gate', 'skill_up', 'skill_down', 'shared_gate', 'shared_up', 'shared_down')}
    del _L3_cond_all
    return {'x': x, 'cond_8': cond_8, 'L0_cond_W_up': _L0_cond_in['W_up'], 'L0_cond_b_up': _L0_cond_in['b_up'], 'L0_cond_W_gate': _L0_cond_in['W_gate'], 'L0_cond_b_gate': _L0_cond_in['b_gate'], 'L0_cond_W_down': _L0_cond_in['W_down'], 'L0_cond_b_down': _L0_cond_in['b_down'], 'L1_cond_W_base': _L1_cond_in['W_base'], 'L1_cond_b_base': _L1_cond_in['b_base'], 'L1_cond_As': _L1_cond_in['As'], 'L1_cond_Bs': _L1_cond_in['Bs'], 'L2_cond_weight': _L2_cond_in['weight'], 'L2_cond_mask': _L2_cond_in['mask'], 'L2_cond_bias': _L2_cond_in['bias'], 'L3_cond_skill_gate': _L3_cond_in['skill_gate'], 'L3_cond_skill_up': _L3_cond_in['skill_up'], 'L3_cond_skill_down': _L3_cond_in['skill_down'], 'L3_cond_shared_gate': _L3_cond_in['shared_gate'], 'L3_cond_shared_up': _L3_cond_in['shared_up'], 'L3_cond_shared_down': _L3_cond_in['shared_down']}

def reference(x, cond_8, L0_cond_W_up, L0_cond_b_up, L0_cond_W_gate, L0_cond_b_gate, L0_cond_W_down, L0_cond_b_down, L1_cond_W_base, L1_cond_b_base, L1_cond_As, L1_cond_Bs, L2_cond_weight, L2_cond_mask, L2_cond_bias, L3_cond_skill_gate, L3_cond_skill_up, L3_cond_skill_down, L3_cond_shared_gate, L3_cond_shared_up, L3_cond_shared_down):
    import jax
    import jax.numpy as jnp

    def _L0_cond_ref(x, opcode_onehot, W_up, b_up, W_gate, b_gate, W_down, b_down):
        import jax, jax.numpy as jnp
        import numpy as np
        B, S, D = (16, 256, 128)
        E, H = (8, 256)
        expert = jnp.argmax(opcode_onehot, axis=-1)
        wu, bu = (W_up[expert], b_up[expert])
        wg, bg = (W_gate[expert], b_gate[expert])
        wd, bd = (W_down[expert], b_down[expert])
        up = jnp.einsum('bsd,bhd->bsh', x, wu) + bu[:, None, :]
        gate = jnp.einsum('bsd,bhd->bsh', x, wg) + bg[:, None, :]
        hidden = jax.nn.silu(up) * gate
        out = jnp.einsum('bsh,bdh->bsd', hidden, wd) + bd[:, None, :]
        return out

    def _L1_cond_ref(x, w, W_base, b_base, As, Bs):
        import jax, jax.numpy as jnp
        import numpy as np
        R = 16
        ALPHA = 32.0
        SCALING = ALPHA / R
        out = jnp.einsum('btc,oc->bto', x, W_base) + b_base
        h = jnp.einsum('btc,erc->bter', x, As)
        lora = jnp.einsum('bter,eor,be->bto', h, Bs, w)
        return out + lora * SCALING

    def _L2_cond_ref(x, y, weight, mask, bias):
        import jax, jax.numpy as jnp
        import numpy as np
        masked_w = weight * mask[None, :, :]
        w_bot = jnp.einsum('bg,got->bot', y, masked_w)
        return jnp.einsum('bnt,bot->bno', x, w_bot) + bias

    def _L3_cond_ref(x, router_logits, skill_gate, skill_up, skill_down, shared_gate, shared_up, shared_down):
        import jax, jax.numpy as jnp
        import numpy as np
        TOP_K = 2
        NUM_MOE_LAYERS = 12

        def _gemma_mlp(x, gate_w, up_w, down_w):
            g = jnp.einsum('bsh,hi->bsi', x, gate_w)
            u = jnp.einsum('bsh,hi->bsi', x, up_w)
            return jnp.einsum('bsi,ih->bsh', jax.nn.gelu(g, approximate=True) * u, down_w)
        B = x.shape[0]
        E = skill_gate.shape[0]
        rw = jax.nn.softmax(router_logits.astype(jnp.float32), axis=-1)
        w, sel = jax.lax.top_k(rw, TOP_K)
        w = w / w.sum(axis=-1, keepdims=True)
        w = w.astype(x.dtype)
        scale = 1.0 / NUM_MOE_LAYERS
        w = scale * w + (1.0 - scale) * jax.lax.stop_gradient(w)
        dense_w = jnp.zeros((B, E), x.dtype).at[jnp.arange(B)[:, None], sel].add(w)

        def step(acc, params):
            g, u, d, we = params
            return (acc + we[:, None, None] * _gemma_mlp(x, g, u, d), None)
        out, _ = jax.lax.scan(step, jnp.zeros_like(x), (skill_gate, skill_up, skill_down, dense_w.T))
        out = out + _gemma_mlp(x, shared_gate, shared_up, shared_down)
        return out
    x = x + _L0_cond_ref(x, cond_8, L0_cond_W_up, L0_cond_b_up, L0_cond_W_gate, L0_cond_b_gate, L0_cond_W_down, L0_cond_b_down)
    x = x + _L1_cond_ref(x, cond_8, L1_cond_W_base, L1_cond_b_base, L1_cond_As, L1_cond_Bs)
    x = x + _L2_cond_ref(x, cond_8, L2_cond_weight, L2_cond_mask, L2_cond_bias)
    x = x + _L3_cond_ref(x, cond_8, L3_cond_skill_gate, L3_cond_skill_up, L3_cond_skill_down, L3_cond_shared_gate, L3_cond_shared_up, L3_cond_shared_down)
    return x

_drawn_inputs = setup_inputs


def setup_inputs(seed=0):
    import zlib

    import numpy as np

    out = dict(_drawn_inputs(seed))
    spreads = {'L0_cond_b_up': (0.0, 0.8), 'L0_cond_b_gate': (0.0, 0.8), 'L0_cond_b_down': (0.0, 0.318)}
    factors = {'L0_cond_W_up': 7.568,
     'L0_cond_W_gate': 7.505,
     'L0_cond_W_down': 6.85,
     'L1_cond_b_base': 11.729,
     'L3_cond_skill_gate': 3.542,
     'L3_cond_skill_up': 3.458,
     'L3_cond_skill_down': 3.399}
    for name, (base, spread) in spreads.items():
        noise = np.random.default_rng([zlib.crc32(name.encode()), seed]).standard_normal(out[name].shape)
        drawn = base * np.exp(spread * noise) if base else spread * noise
        out[name] = jnp.asarray(drawn.astype(out[name].dtype))
    for name, factor in factors.items():
        out[name] = (out[name] * factor).astype(out[name].dtype)
    return out
```

```python
from contextlib import ExitStack

import concourse.bass as bass
from concourse import mybir

ALU = mybir.AluOpType
ACT = mybir.ActivationFunctionType
F32 = mybir.dt.float32
F32R = mybir.dt.float32r
U32 = mybir.dt.uint32

P = 128
B = 16
E = 8
R = 16
H0 = 256
H3 = 512
K = 2
LORA_SCALE = 32.0 / R
W_SCALE = 1.0 / 12

C0 = H0 // P
C3 = H3 // P
GB = 4
G = B // GB
N = GB * P

UP0, GATE0, DOWN0 = 0, H0, 2 * H0
BUP0, BGATE0, BDOWN0 = 3 * H0, 3 * H0 + C0, 3 * H0 + 2 * C0
PACK0 = BDOWN0 + 1
GATE3, UP3, DOWN3 = 0, H3, 2 * H3
PACK3 = 3 * H3
BS1, AS1, BASE1, MASK2, DELTA, BIAS1, BIAS2 = 0, P, 2 * P, 3 * P, 4 * P, 4 * P + B, 4 * P + B + 1
SMALL = BIAS2 + 1

SLOTS0 = GB
SLOTS3 = GB * K

ORDER = [u for c in range(GB) for u in (("S", c), ("R", c, 0), ("R", c, 1))]
UNITS = len(ORDER)
PAIRS = 3
AHEAD = 2
FREE = 2
HID3 = FREE + B
assert C3 == GB and UNITS % PAIRS == 0


def build_kernel(nc, xT, cond, condT, small, w2, experts0, experts3, shared, out):
    ctx = ExitStack()
    with ctx:
        def sb(name, shape, dt=F32):
            return ctx.enter_context(nc.sbuf_tensor(name, shape, dt))

        def sem(name):
            return ctx.enter_context(nc.semaphore(name))

        x = sb("x", [P, B * P])
        x_hi = sb("x_hi", [P, B * P], F32R)
        x_lo = sb("x_lo", [P, B * P], F32R)
        ring0 = sb("ring0", [P, SLOTS0, PACK0])
        ring3 = sb("ring3", [P, SLOTS3, PACK3])
        small_sb = sb("small_sb", [P, SMALL])
        w2_sb = sb("w2_sb", [P, E, P])
        shared_sb = sb("shared_sb", [P, PACK3])
        shared_hi = sb("shared_hi", [P, PACK3], F32R)
        shared_lo = sb("shared_lo", [P, PACK3], F32R)
        cond_sb = sb("cond_sb", [B, E + B])
        cond_rep = sb("cond_rep", [P, B])
        ones = sb("ones", [B, P])
        top = sb("top", [B, E])
        top_at = sb("top_at", [B, E], U32)
        neg_max = sb("neg_max", [B, 1])
        expd = sb("expd", [B, E])
        expsum = sb("expsum", [B, 1])
        inv = sb("inv", [B, 2])
        probs = sb("probs", [B, K])
        pair_sum = sb("pair_sum", [B, 1])
        pw = sb("pw", [B, K])
        pw_rest = sb("pw_rest", [B, K])
        pw_all = sb("pw_all", [B, K])
        at_diag = sb("at_diag", [B, K, B])
        pw_diag = sb("pw_diag", [B, K, B])
        at_row = sb("at_row", [1, K * B], U32)
        w_col = sb("w_col", [P, K * B])
        bs_w = sb("bs_w", [P, B, P])
        y_delta = sb("y_delta", [P, B, R])
        lora_raw = sb("lora_raw", [P, B, P])
        lin1 = sb("lin1", [P, B, P])
        mix_raw = sb("mix_raw", [P, E, B, R])
        lin2 = sb("lin2", [P, B, P])
        act0 = sb("act0", [P, FREE, C0, P])
        hid0 = sb("hid0", [P, FREE, C0, P])
        act3 = sb("act3", [P, PAIRS, N])
        hid3 = sb("hid3", [P, PAIRS, N])
        hid_hi = sb("hid_hi", [P, N], F32R)
        hid_lo = sb("hid_lo", [P, N], F32R)

        pair = [[ctx.enter_context(nc.psum_tensor(f"pair{p}_{n}", [P, N], F32)) for n in range(2)]
                for p in range(PAIRS)]
        acc = [ctx.enter_context(nc.psum_tensor(f"acc{n}", [P, N], F32)) for n in range(2)]
        lin = pair[PAIRS - 1]

        cond_in, rep_in, small_in, w2_in = sem("cond_in"), sem("rep_in"), sem("small_in"), sem("w2_in")
        x_in, shared_in = sem("x_in"), sem("shared_in")
        e0_in = [sem(f"e0_in{n}") for n in range(SLOTS0)]
        e3_in = [sem(f"e3_in{n}") for n in range(SLOTS3)]
        stored = sem("stored")
        route = sem("route")
        ones_set = sem("ones_set")
        exp_done = sem("exp_done")
        at_diag_done, at_mm, at_done = sem("at_diag_done"), sem("at_mm"), sem("at_done")
        pw_diag_done, pw_mm, pw_done = sem("pw_diag_done"), sem("pw_mm"), sem("pw_done")
        ydelta_done, bsw_done = sem("ydelta_done"), sem("bsw_done")
        prep_mm = sem("prep_mm")
        prep_copied = sem("prep_copied")
        lin2_done, lin1_done = sem("lin2_done"), sem("lin1_done")
        shared_hi_done, shared_done = sem("shared_hi_done"), sem("shared_done")
        gu_done, act_done, hid_done = sem("gu_done"), sem("act_done"), sem("hid_done")
        down0_done, x1_done = sem("down0_done"), sem("x1_done")
        lin_mm, lin_read = sem("lin_mm"), sem("lin_read")
        x_hi_done, x_lo_done = sem("x_hi_done"), sem("x_lo_done")
        split = sem("split")
        down3_done, y_done = sem("down3_done"), sem("y_done")

        block = ctx.enter_context(nc.Block())

        def cols(b):
            return bass.ds(b * P, P)

        def group(g):
            return bass.ds(g * N, N)

        @block.sync
        def _(sp):
            sp.dma_start(cond_sb[:, :], cond).then_inc(cond_in, 16)
            sp.dma_start(small_sb[:, :], small).then_inc(small_in, 16)

            def load0(b, j):
                at = sp.value_load(at_row[0:1, bass.ds(b, 1)], min_val=0, max_val=E - 1)
                sp.dma_start(ring0[:, j, :], experts0[bass.ds(at, 1), :, :].rearrange("e p n -> p (e n)"))\
                  .then_inc(e0_in[j], 16)

            def load3(g, c, k):
                at = sp.value_load(at_row[0:1, bass.ds(g * GB + (k * B + c), 1)], min_val=0, max_val=E - 1)
                slot = c * K + k
                sp.dma_start(ring3[:, slot, :], experts3[bass.ds(at, 1), :, :].rearrange("e p n -> p (e n)"))\
                  .then_inc(e3_in[slot], 16)

            sp.wait_ge(at_done, 1)
            for j in range(SLOTS0):
                load0(j, j)
            with sp.Fori(0, G - 1) as g:
                for j in range(GB):
                    sp.wait_ge(x1_done, g * GB + (j + 1))
                    load0(g * GB + (GB + j), j)
            sp.dma_start(shared_sb[:, :], shared).then_inc(shared_in, 16)
            for c in range(GB):
                for k in range(K):
                    load3(0, c, k)
            with sp.Fori(1, G) as g:
                for u, (kind, *at) in enumerate(ORDER):
                    if kind == "R":
                        sp.wait_ge(down3_done, g * UNITS + (u + 1 - UNITS))
                        load3(g, *at)
                sp.wait_ge(y_done, g + 1)
                sp.dma_start(out[:, group(g - 1)], x[:, group(g - 1)]).then_inc(stored, 16)
            sp.wait_ge(y_done, G + 1)
            sp.dma_start(out[:, group(G - 1)], x[:, group(G - 1)]).then_inc(stored, 16)
            sp.wait_ge(stored, 16 * G)

        @block.gpsimd
        def _(pool):
            pool.memset(ones[:, :], 1.0).then_inc(ones_set, 1)
            for k in range(E):
                if k % 2 == 0:
                    pool.wait_ge(prep_copied, k // 2 + 1)
                dst = lin2[:, :, k * R:(k + 1) * R]
                mask = small_sb[:, MASK2 + k * R:MASK2 + (k + 1) * R].unsqueeze(1).to_broadcast([P, B, R])
                pool.tensor_tensor(dst, mix_raw[:, k, :, :], mask, ALU.mult).then_inc(lin2_done, 1)
            for q in range(G):
                pool.wait_ge(prep_copied, E // 2 + q + 1)
                base = small_sb[:, BASE1:BASE1 + P].unsqueeze(1).to_broadcast([P, GB, P])
                at = slice(q * GB, (q + 1) * GB)
                pool.tensor_tensor(lin1[:, at, :], lora_raw[:, at, :], base, ALU.add).then_inc(lin1_done, 1)
            pool.wait_ge(shared_in, 16)
            pool.tensor_copy(shared_hi[:, :], shared_sb[:, :]).then_inc(shared_hi_done, 1)
            pool.wait_ge(shared_hi_done, 1)
            pool.tensor_tensor(shared_lo[:, :], shared_sb[:, :], shared_hi[:, :].bitcast(F32), ALU.subtract)\
                .then_inc(shared_done, 1)

        @block.scalar
        def _(act):
            rep = condT.unsqueeze(1).to_broadcast([E, R, B])
            act.dma_start(cond_rep[:, :], rep).then_inc(rep_in, 16)
            act.dma_start(w2_sb[:, :, :], w2).then_inc(w2_in, 16)
            act.dma_start(x[:, :], xT).then_inc(x_in, 16)
            act.wait_ge(route, 2)
            act.activation(expd[:, :], top[:, :], ACT.Exp, bias=neg_max[:, 0:1], accum_out=expsum[:, 0:1])\
               .then_inc(exp_done, 1)
            for n in range(E // 2 + G):
                act.wait_ge(prep_mm, n + 1)
                if n < E // 2:
                    dst = mix_raw[:, 2 * n:2 * n + 2, :, :].rearrange("p k b j -> p (k b j)")
                else:
                    q = n - E // 2
                    dst = lora_raw[:, q * GB:(q + 1) * GB, :].rearrange("p b o -> p (b o)")
                act.activation(dst, lin[n % 2][:, :], ACT.Copy).then_inc(prep_copied, 1)

            with act.Fori(0, G) as g:
                for j in range(GB):
                    act.wait_ge(gu_done, g * GB + (j + 1))
                    for c in range(C0):
                        ins = act.activation(act0[:, j % FREE, c, :], pair[j % FREE][0][:, c * P:(c + 1) * P],
                                             ACT.Silu, bias=ring0[:, j, BUP0 + c:BUP0 + c + 1])
                    ins.then_inc(act_done, 1)
            for g in range(G):
                act.wait_ge(lin_read, G + g + 1)
                act.activation(x_hi[:, group(g)], x[:, group(g)], ACT.Copy).then_inc(x_hi_done, 1)
            with act.Fori(0, G) as g:
                for u in range(UNITS):
                    act.wait_ge(gu_done, g * UNITS + (B + u + 1))
                    act.activation(act3[:, u % PAIRS, :], pair[u % PAIRS][0][:, :], ACT.Gelu_apprx_tanh)\
                       .then_inc(act_done, 1)

        @block.tensor
        def _(pe):
            pe.wait_ge(ones_set, 1)
            pe.wait_ge(at_diag_done, 1)
            pe.matmul(acc[1][:, 0:K * B], ones[:, :], at_diag[:, :, :].rearrange("b k n -> b (k n)"),
                      start=True, stop=True).then_inc(at_mm, 1)
            pe.wait_ge(ydelta_done, 1)
            pe.wait_ge(w2_in, 16)
            for k in range(E):
                n = k // 2
                if k % 2 == 0 and n >= 2:
                    pe.wait_ge(prep_copied, n - 1)
                ins = pe.matmul(lin[n % 2][:, (k % 2) * B * R:(k % 2 + 1) * B * R], w2_sb[:, k, :],
                                y_delta[:, :, :].rearrange("p b j -> p (b j)"), start=True, stop=True)
                if k % 2 == 1:
                    ins.then_inc(prep_mm, 1)
            for q in range(G):
                n = E // 2 + q
                pe.wait_ge(bsw_done, q + 1)
                pe.wait_ge(prep_copied, n - 1)
                pe.matmul(lin[n % 2][:, :], small_sb[:, AS1:AS1 + P],
                          bs_w[:, q * GB:(q + 1) * GB, :].rearrange("p b o -> p (b o)"),
                          start=True, stop=True).then_inc(prep_mm, 1)
            pe.wait_ge(at_done, 1)
            pe.wait_ge(pw_diag_done, 1)
            pe.matmul(acc[1][:, 0:K * B], ones[:, :], pw_diag[:, :, :].rearrange("b k n -> b (k n)"),
                      start=True, stop=True).then_inc(pw_mm, 1)

            def upgate0(g, j):
                pe.wait_ge(e0_in[j], g * 16 + 16)
                pe.wait_ge(hid_done, g * GB + (j + 1))
                for half, base in enumerate((UP0, GATE0)):
                    for c in range(C0):
                        ins = pe.matmul(pair[j % FREE][half][:, c * P:(c + 1) * P],
                                        ring0[:, j, base + c * P:base + (c + 1) * P],
                                        x[:, cols(g * GB + j)], start=True, stop=True)
                ins.then_inc(gu_done, 1)

            def down0(g, j):
                pe.wait_ge(hid_done, g * GB + (FREE + j + 1))
                for c in range(C0):
                    ins = pe.matmul(acc[j % 2][:, 0:P], ring0[:, j, DOWN0 + c * P:DOWN0 + (c + 1) * P],
                                    hid0[:, j % FREE, c, :], start=(c == 0), stop=(c == C0 - 1))
                ins.then_inc(down0_done, 1)

            def layer0(g, last):
                for j in range(GB):
                    if j + 1 < GB:
                        upgate0(g, j + 1)
                    elif not last:
                        upgate0(g + 1, 0)
                    down0(g, j)

            pe.wait_ge(pw_done, 1)
            pe.wait_ge(x_in, 16)
            upgate0(0, 0)
            with pe.Fori(0, G - 1) as g:
                layer0(g, False)
            layer0(G - 1, True)

            pe.wait_ge(lin1_done, G)
            pe.wait_ge(prep_copied, E // 2 + G)
            for g in range(G):
                pe.wait_ge(x1_done, GB * (g + 1))
                if g >= 2:
                    pe.wait_ge(lin_read, g - 1)
                for j in range(GB):
                    ins = pe.matmul(lin[g % 2][:, j * P:(j + 1) * P], lin1[:, g * GB + j, :],
                                    x[:, cols(g * GB + j)], start=True, stop=True)
                ins.then_inc(lin_mm, 1)
            pe.wait_ge(lin2_done, E)
            for g in range(G):
                pe.wait_ge(lin_read, G - 1 + g)
                for j in range(GB):
                    ins = pe.matmul(lin[g % 2][:, j * P:(j + 1) * P], lin2[:, g * GB + j, :],
                                    x[:, cols(g * GB + j)], start=True, stop=True)
                ins.then_inc(lin_mm, 1)

            def gateup3(g, u):
                kind, c, *k = ORDER[u]
                gate, up = pair[u % PAIRS]
                if kind == "S":
                    pe.wait_ge(x_lo_done, g + 1)
                    for bank, base in ((gate, GATE3), (up, UP3)):
                        at = slice(base + c * P, base + (c + 1) * P)
                        for n, (w, v) in enumerate(((shared_hi, x_hi), (shared_hi, x_lo), (shared_lo, x_hi))):
                            ins = pe.matmul(bank[:, :], w[:, at], v[:, group(g)], start=(n == 0), stop=(n == 2))
                else:
                    slot = c * K + k[0]
                    pe.wait_ge(e3_in[slot], g * 16 + 16)
                    for bank, base in ((gate, GATE3), (up, UP3)):
                        for m in range(C3):
                            ins = pe.matmul(bank[:, m * P:(m + 1) * P],
                                            ring3[:, slot, base + m * P:base + (m + 1) * P],
                                            x[:, cols(g * GB + c)], start=True, stop=True)
                ins.then_inc(gu_done, 1)

            def down3(g, u):
                kind, c, *k = ORDER[u]
                y = acc[0]
                pe.wait_ge(hid_done, g * UNITS + (HID3 + u + 1))
                if kind == "S":
                    at = slice(DOWN3 + c * P, DOWN3 + (c + 1) * P)
                    for n, (w, v) in enumerate(((shared_hi, hid_hi), (shared_hi, hid_lo), (shared_lo, hid_hi))):
                        ins = pe.matmul(y[:, :], w[:, at], v[:, :], start=(u == 0 and n == 0), stop=False,
                                        skip_group_check=True)
                else:
                    for m in range(C3):
                        ins = pe.matmul(y[:, c * P:(c + 1) * P],
                                        ring3[:, c * K + k[0], DOWN3 + m * P:DOWN3 + (m + 1) * P],
                                        hid3[:, u % PAIRS, m * P:(m + 1) * P], start=False,
                                        stop=(u == UNITS - 1 and m == C3 - 1), skip_group_check=True)
                ins.then_inc(down3_done, 1)

            def layer3(g, last):
                for u in range(UNITS):
                    ahead = u + AHEAD
                    if ahead < UNITS or not last:
                        pe.wait_ge(hid_done, g * UNITS + (HID3 + ahead - PAIRS + 1))
                        gateup3(g + ahead // UNITS, ahead % UNITS)
                    if u == 0:
                        pe.wait_ge(y_done, g + 1)
                    down3(g, u)

            pe.wait_ge(hid_done, HID3)
            pe.wait_ge(x1_done, B)
            pe.wait_ge(shared_done, 1)
            gateup3(0, 0)
            gateup3(0, 1)
            pe.wait_ge(lin_read, 2 * G)
            with pe.Fori(0, G - 1) as g:
                layer3(g, False)
            layer3(G - 1, True)

        @block.vector
        def _(dve):
            eye = cond_sb[:, E:E + B]

            dve.memset(inv[:, :], 0.0).then_inc(hid_done, FREE)
            dve.memset(expsum[:, :], 0.0).then_inc(y_done, 1)
            dve.wait_ge(cond_in, 16)
            dve.max(top[:, :], cond_sb[:, 0:E]).then_inc(route, 1)
            dve.wait_ge(route, 1)
            dve.tensor_scalar(neg_max[:, :], top[:, 0:1], -1.0, None, ALU.mult).then_inc(route, 1)
            dve.max_index(top_at[:, :], top[:, :], cond_sb[:, 0:E]).then_inc(route, 1)
            dve.wait_ge(route, 3)

            def diagonal(dst, src):
                return dve.tensor_tensor(dst[:, :, :], src[:, 0:K].unsqueeze(2).to_broadcast([B, K, B]),
                                         eye.unsqueeze(1).to_broadcast([B, K, B]), ALU.mult)

            diagonal(at_diag, top_at).then_inc(at_diag_done, 1)
            dve.wait_ge(at_mm, 1)
            dve.tensor_copy(at_row[:, :], acc[1][0:1, 0:K * B]).then_inc(at_done, 1)

            dve.wait_ge(rep_in, 16)
            dve.wait_ge(small_in, 16)
            dve.tensor_tensor(y_delta[:, :, :], cond_rep[:, :].unsqueeze(2).to_broadcast([P, B, R]),
                              small_sb[:, DELTA:DELTA + R].unsqueeze(1).to_broadcast([P, B, R]), ALU.mult)\
               .then_inc(ydelta_done, 1)
            for q in range(G):
                at = slice(q * GB, (q + 1) * GB)
                dve.scalar_tensor_tensor(
                    bs_w[:, at, :], small_sb[:, BS1:BS1 + P].unsqueeze(1).to_broadcast([P, GB, P]), LORA_SCALE,
                    cond_rep[:, at].unsqueeze(2).to_broadcast([P, GB, P]), ALU.mult, ALU.mult)\
                   .then_inc(bsw_done, 1)

            step = [3]

            def chained(ins):
                step[0] += 1
                ins.then_inc(route, 1)
                dve.wait_ge(route, step[0])

            dve.wait_ge(exp_done, 1)
            chained(dve.reciprocal(inv[:, 0:1], expsum[:, :]))
            chained(dve.tensor_scalar(probs[:, :], expd[:, 0:K], inv[:, 0:1], None, ALU.mult))
            chained(dve.tensor_tensor(pair_sum[:, :], probs[:, 0:1], probs[:, 1:2], ALU.add))
            chained(dve.reciprocal(inv[:, 1:2], pair_sum[:, :]))
            chained(dve.tensor_scalar(pw[:, :], probs[:, :], inv[:, 1:2], None, ALU.mult))
            chained(dve.tensor_scalar(pw_rest[:, :], pw[:, :], 1.0 - W_SCALE, None, ALU.mult))
            chained(dve.scalar_tensor_tensor(pw_all[:, :], pw[:, :], W_SCALE, pw_rest[:, :], ALU.mult, ALU.add))
            diagonal(pw_diag, pw_all).then_inc(pw_diag_done, 1)
            dve.wait_ge(pw_mm, 1)
            dve.tensor_copy(w_col[:, :], acc[1][:, 0:K * B]).then_inc(pw_done, 1)

            dve.wait_ge(x_in, 16)
            with dve.Fori(0, G) as g:
                for j in range(GB):
                    dve.wait_ge(act_done, g * GB + (j + 1))
                    for c in range(C0):
                        ins = dve.scalar_tensor_tensor(
                            hid0[:, j % FREE, c, :], pair[j % FREE][1][:, c * P:(c + 1) * P],
                            ring0[:, j, BGATE0 + c:BGATE0 + c + 1], act0[:, j % FREE, c, :], ALU.add, ALU.mult)
                    ins.then_inc(hid_done, 1)
                    dve.wait_ge(down0_done, g * GB + (j + 1))
                    dve.scalar_tensor_tensor(x[:, cols(g * GB + j)], acc[j % 2][:, 0:P],
                                             ring0[:, j, BDOWN0:BDOWN0 + 1], x[:, cols(g * GB + j)],
                                             ALU.add, ALU.add).then_inc(x1_done, 1)

            def linear(n, g):
                dve.wait_ge(lin_mm, n + 1)
                bias = small_sb[:, BIAS1:BIAS1 + 1] if n < G else small_sb[:, BIAS2:BIAS2 + 1]
                dve.scalar_tensor_tensor(x[:, group(g)], lin[n % 2][:, :], bias, x[:, group(g)],
                                         ALU.add, ALU.add).then_inc(lin_read, 1)

            def low_part(g):
                dve.wait_ge(x_hi_done, g + 1)
                dve.tensor_tensor(x_lo[:, group(g)], x[:, group(g)], x_hi[:, group(g)].bitcast(F32),
                                  ALU.subtract).then_inc(x_lo_done, 1)

            dve.wait_ge(x1_done, B)
            for g in range(G):
                linear(g, g)
            dve.wait_ge(lin_read, G)
            for g in range(G):
                linear(G + g, g)
                if g:
                    low_part(g - 1)
            low_part(G - 1)

            def hidden(g, u):
                kind, c, *k = ORDER[u]
                s = u % PAIRS
                dve.wait_ge(act_done, g * UNITS + (B + u + 1))
                if kind == "R":
                    dve.scalar_tensor_tensor(hid3[:, s, :], pair[s][1][:, :],
                                             w_col[:, bass.ds(g * GB + (k[0] * B + c), 1)], act3[:, s, :],
                                             ALU.mult, ALU.mult).then_inc(hid_done, 1)
                    return
                dve.tensor_tensor(hid3[:, s, :], pair[s][1][:, :], act3[:, s, :], ALU.mult).then_inc(split, 1)
                dve.wait_ge(split, g * (2 * GB) + (2 * c + 1))
                dve.tensor_copy(hid_hi[:, :], hid3[:, s, :]).then_inc(split, 1)
                dve.wait_ge(split, g * (2 * GB) + (2 * c + 2))
                dve.tensor_tensor(hid_lo[:, :], hid3[:, s, :], hid_hi[:, :].bitcast(F32), ALU.subtract)\
                   .then_inc(hid_done, 1)

            def result(g):
                dve.wait_ge(down3_done, g * UNITS + UNITS)
                dve.tensor_tensor(x[:, group(g)], acc[0][:, :], x[:, group(g)], ALU.add).then_inc(y_done, 1)

            for u in range(UNITS):
                hidden(0, u)
            with dve.Fori(1, G) as g:
                for u in range(UNITS):
                    if u == AHEAD:
                        result(g - 1)
                    hidden(g, u)
            result(G - 1)


def kernel(x, cond_8, L0_cond_W_up, L0_cond_b_up, L0_cond_W_gate, L0_cond_b_gate, L0_cond_W_down, L0_cond_b_down,
           L1_cond_W_base, L1_cond_b_base, L1_cond_As, L1_cond_Bs, L2_cond_weight, L2_cond_mask, L2_cond_bias,
           L3_cond_skill_gate, L3_cond_skill_up, L3_cond_skill_down, L3_cond_shared_gate, L3_cond_shared_up,
           L3_cond_shared_down):
    import numpy as np
    import concourse.bacc as bacc
    from concourse.bass_utils import run_bass_kernel_spmd

    def arr(a):
        return np.asarray(a)

    def experts(parts):
        return np.ascontiguousarray(np.concatenate(parts, axis=-1))

    def down_rows(w, chunks):
        lead = w.shape[:-2]
        n = len(lead)
        w = w.reshape(*lead, chunks, P, P)
        return w.transpose(*range(n), n + 1, n, n + 2).reshape(*lead, P, chunks * P)

    def bias_cols(b, chunks):
        return arr(b).reshape(E, chunks, P).transpose(0, 2, 1)

    arrays = {
        "xT": np.ascontiguousarray(arr(x).transpose(2, 0, 1).reshape(P, B * P)),
        "cond": experts([arr(cond_8), np.eye(B, dtype=np.float32)]),
        "condT": np.ascontiguousarray(arr(cond_8).T),
        "small": experts([
            arr(L1_cond_Bs).transpose(0, 2, 1).reshape(E * R, P),
            arr(L1_cond_As).reshape(E * R, P),
            arr(L1_cond_W_base).T,
            arr(L2_cond_mask).T,
            np.tile(np.eye(R, dtype=np.float32), (E, 1)),
            arr(L1_cond_b_base).reshape(P, 1),
            arr(L2_cond_bias).reshape(P, 1),
        ]),
        "w2": np.ascontiguousarray(
            arr(L2_cond_weight).reshape(E, P // R, R, P).transpose(0, 2, 1, 3).reshape(E * R, P // R, P)),
        "experts0": experts([
            arr(L0_cond_W_up).transpose(0, 2, 1),
            arr(L0_cond_W_gate).transpose(0, 2, 1),
            down_rows(arr(L0_cond_W_down).transpose(0, 2, 1), C0),
            bias_cols(L0_cond_b_up, C0),
            bias_cols(L0_cond_b_gate, C0),
            bias_cols(L0_cond_b_down, 1),
        ]),
        "experts3": experts([arr(L3_cond_skill_gate), arr(L3_cond_skill_up), down_rows(arr(L3_cond_skill_down), C3)]),
        "shared": experts([arr(L3_cond_shared_gate), arr(L3_cond_shared_up), down_rows(arr(L3_cond_shared_down), C3)]),
    }
    nc = bacc.Bacc("TRN2", target_bir_lowering=False, num_devices=1)
    args = [nc.dram_tensor(n, a.shape, mybir.dt.from_np(a.dtype), kind="ExternalInput").ap()
            for n, a in arrays.items()]
    args.append(nc.dram_tensor("out", (P, B * P), F32, kind="ExternalOutput").ap())
    build_kernel(nc, *args)
    r = run_bass_kernel_spmd(nc, [arrays], core_ids=[0])
    return r.results[0]["out"].reshape(P, B, P).transpose(1, 2, 0)
```

```python
from contextlib import ExitStack

import concourse.bass as bass
from concourse import mybir

ALU = mybir.AluOpType
ACT = mybir.ActivationFunctionType
F32 = mybir.dt.float32
F32R = mybir.dt.float32r
U32 = mybir.dt.uint32
BF16 = mybir.dt.bfloat16

P = 128
B = 16
E = 8
R = 16
H0 = 256
H3 = 512
K = 2
LORA_SCALE = 32.0 / R
W_SCALE = 1.0 / 12

C0 = H0 // P
C3 = H3 // P
GB = 4
G = B // GB
N = GB * P

UP0, GATE0, DOWN0 = 0, H0, 2 * H0
BUP0, BGATE0, BDOWN0 = 3 * H0, 3 * H0 + C0, 3 * H0 + 2 * C0
PACK0 = BDOWN0 + 1
GATE3, UP3, DOWN3 = 0, H3, 2 * H3
PACK3 = 3 * H3
BASE1, MASK2, DELTA, BIAS1, BIAS2 = 0, P, 2 * P, 2 * P + B, 2 * P + B + 1
SMALL = BIAS2 + 1
BS1, AS1 = 0, P

SLOTS0 = 8
SLOTS3 = GB * K

ORDER = [u for c in range(GB) for u in (("S", c), ("R", c, 0), ("R", c, 1))]
UNITS = len(ORDER)
MAIN = ORDER.index(("S", GB - 1))
LAST = ORDER.index(("R", GB - 1, 0))
PAIRS = 3
AHEAD = 2
FREE = 2
STEPS0 = B // SLOTS0
ACT3 = B * C0
HID3 = (FREE + B) * C0
assert C3 == GB and UNITS % PAIRS == 0


def build_kernel(nc, xT, cond, condT, lora, small, w2, experts0, experts3, shared, out):
    ctx = ExitStack()
    with ctx:
        def sb(name, shape, dt=F32):
            return ctx.enter_context(nc.sbuf_tensor(name, shape, dt))

        def sem(name):
            return ctx.enter_context(nc.semaphore(name))

        x = sb("x", [P, B * P])
        x_hi = sb("x_hi", [P, B * P], F32R)
        x_lo = sb("x_lo", [P, B * P], F32R)
        ring0 = sb("ring0", [P, SLOTS0, PACK0])
        ring3 = sb("ring3", [P, SLOTS3, PACK3])
        lora_sb = sb("lora_sb", [P, 2 * P])
        small_sb = sb("small_sb", [P, SMALL])
        w2_sb = sb("w2_sb", [P, E, P])
        shared_sb = sb("shared_sb", [P, PACK3])
        shared_hi = sb("shared_hi", [P, PACK3], F32R)
        shared_lo = sb("shared_lo", [P, PACK3], F32R)
        cond_sb = sb("cond_sb", [B, E + B])
        cond_rep = sb("cond_rep", [P, B])
        ones = sb("ones", [B, P])
        zeros = sb("zeros", [P, N], BF16)
        top = sb("top", [B, E])
        top_at = sb("top_at", [B, E], U32)
        neg_max = sb("neg_max", [B, 1])
        expd = sb("expd", [B, E])
        expsum = sb("expsum", [B, 1])
        inv = sb("inv", [B, 2])
        probs = sb("probs", [B, K])
        pair_sum = sb("pair_sum", [B, 1])
        pw = sb("pw", [B, K])
        pw_rest = sb("pw_rest", [B, K])
        pw_all = sb("pw_all", [B, K])
        at_diag = sb("at_diag", [B, K, B])
        pw_diag = sb("pw_diag", [B, K, B])
        at_row = sb("at_row", [1, K * B], U32)
        w_col = sb("w_col", [P, K * B])
        bs_w = sb("bs_w", [P, B, P])
        y_delta = sb("y_delta", [P, B, R])
        lora_raw = sb("lora_raw", [P, B, P])
        lin1 = sb("lin1", [P, B, P])
        mix_raw = sb("mix_raw", [P, E, B, R])
        lin2 = sb("lin2", [P, B, P])
        act0 = sb("act0", [P, FREE, C0, P])
        hid0 = sb("hid0", [P, FREE, C0, P])
        act3 = sb("act3", [P, PAIRS, N])
        hid3 = sb("hid3", [P, PAIRS, N])
        hid_hi = sb("hid_hi", [P, N], F32R)
        hid_lo = sb("hid_lo", [P, N], F32R)

        pair = [[ctx.enter_context(nc.psum_tensor(f"pair{p}_{n}", [P, N], F32)) for n in range(2)]
                for p in range(PAIRS)]
        acc = [ctx.enter_context(nc.psum_tensor(f"acc{n}", [P, N], F32)) for n in range(2)]
        lin = pair[PAIRS - 2] + pair[PAIRS - 1]
        prep = pair[PAIRS - 1]
        assert len(lin) == G

        cond_in, rep_in, lora_in = sem("cond_in"), sem("rep_in"), sem("lora_in")
        small_in, w2_in = sem("small_in"), sem("w2_in")
        x_in, shared_in = sem("x_in"), sem("shared_in")
        e0_in = [sem(f"e0_in{n}") for n in range(SLOTS0)]
        e3_in = [sem(f"e3_in{n}") for n in range(SLOTS3)]
        stored = sem("stored")
        route = sem("route")
        ones_set, zeros_set = sem("ones_set"), sem("zeros_set")
        exp_done = sem("exp_done")
        at_diag_done, at_mm, at_done = sem("at_diag_done"), sem("at_mm"), sem("at_done")
        pw_diag_done, pw_mm, pw_done = sem("pw_diag_done"), sem("pw_mm"), sem("pw_done")
        ydelta_done, bsw_done = sem("ydelta_done"), sem("bsw_done")
        prep_mm = sem("prep_mm")
        prep_copied = sem("prep_copied")
        lin2_done, lin1_done = sem("lin2_done"), sem("lin1_done")
        shared_hi_done, shared_done = sem("shared_hi_done"), sem("shared_done")
        inner_done, outer_done = sem("inner_done"), sem("outer_done")
        act_done, hid_done = sem("act_done"), sem("hid_done")
        down0_done, x1_done = sem("down0_done"), sem("x1_done")
        lin_mm, lin_read = sem("lin_mm"), sem("lin_read")
        x_hi_done, x_lo_done = sem("x_hi_done"), sem("x_lo_done")
        split = sem("split")
        down3_done = sem("down3_done")
        ymain_done, ylast_done = sem("ymain_done"), sem("ylast_done")

        block = ctx.enter_context(nc.Block())

        def cols(b):
            return bass.ds(b * P, P)

        def x1_value(b):
            return b + (SLOTS0 + 1)

        def group(g):
            return bass.ds(g * N, N)

        @block.sync
        def _(sp):
            sp.dma_start(cond_sb[:, :], cond).then_inc(cond_in, 16)
            sp.dma_start(lora_sb[:, :], lora).then_inc(lora_in, 16)
            sp.dma_start(w2_sb[:, :, :], w2).then_inc(w2_in, 16)

            def load0(b, j):
                at = sp.value_load(at_row[0:1, bass.ds(b, 1)], min_val=0, max_val=E - 1)
                sp.wait_ge(x1_done, b + 1)
                sp.dma_start(ring0[:, j, :], experts0[bass.ds(at, 1), :, :].rearrange("e p n -> p (e n)"))\
                  .then_inc(e0_in[j], 16)

            def load3(g, u, first=False):
                _, c, k = ORDER[u]
                at = sp.value_load(at_row[0:1, bass.ds(g * GB + (k * B + c), 1)], min_val=0, max_val=E - 1)
                slot = c * K + k
                if not first:
                    sp.wait_ge(down3_done, g * UNITS + (u + 1 - UNITS))
                sp.dma_start(ring3[:, slot, :], experts3[bass.ds(at, 1), :, :].rearrange("e p n -> p (e n)"))\
                  .then_inc(e3_in[slot], 16)

            def store3(g):
                sp.wait_ge(ymain_done, g + 2)
                at = bass.ds(g * N, N - P)
                sp.dma_start(out[:, at], x[:, at]).then_inc(stored, 16)
                sp.wait_ge(ylast_done, g + 2)
                at = cols(g * GB + (GB - 1))
                sp.dma_start(out[:, at], x[:, at]).then_inc(stored, 16)

            sp.wait_ge(at_done, 1)
            with sp.Fori(0, STEPS0) as s:
                for j in range(SLOTS0):
                    load0(s * SLOTS0 + j, j)
            routed = [u for u in range(UNITS) if ORDER[u][0] == "R"]
            for u in routed:
                load3(0, u, first=True)
            with sp.Fori(1, G) as g:
                for u in routed:
                    load3(g, u)
                store3(g - 1)
            store3(G - 1)
            sp.wait_ge(stored, 16 * 2 * G)

        @block.gpsimd
        def _(pool):
            pool.memset(zeros[:, :], 0.0).then_inc(zeros_set, 1)
            pool.memset(ones[:, :], 1.0).then_inc(ones_set, 1)
            pool.wait_ge(small_in, 16)
            for q in range(G):
                pool.wait_ge(prep_copied, q + 1)
                base = small_sb[:, BASE1:BASE1 + P].unsqueeze(1).to_broadcast([P, GB, P])
                at = slice(q * GB, (q + 1) * GB)
                pool.tensor_tensor(lin1[:, at, :], lora_raw[:, at, :], base, ALU.add).then_inc(lin1_done, 1)
            for k in range(E):
                if k % 2 == 0:
                    pool.wait_ge(prep_copied, G + k // 2 + 1)
                dst = lin2[:, :, k * R:(k + 1) * R]
                mask = small_sb[:, MASK2 + k * R:MASK2 + (k + 1) * R].unsqueeze(1).to_broadcast([P, B, R])
                pool.tensor_tensor(dst, mix_raw[:, k, :, :], mask, ALU.mult).then_inc(lin2_done, 1)
            pool.wait_ge(shared_in, 16)
            pool.tensor_copy(shared_hi[:, :], shared_sb[:, :]).then_inc(shared_hi_done, 1)
            pool.wait_ge(shared_hi_done, 1)
            pool.tensor_tensor(shared_lo[:, :], shared_sb[:, :], shared_hi[:, :].bitcast(F32), ALU.subtract)\
                .then_inc(shared_done, 1)

        @block.scalar
        def _(act):
            rep = condT.unsqueeze(1).to_broadcast([E, R, B])
            act.dma_start(cond_rep[:, :], rep).then_inc(rep_in, 16)
            act.dma_start(small_sb[:, :], small).then_inc(small_in, 16)
            act.dma_start(x[:, :], xT).then_inc(x_in, 16)
            act.dma_start(shared_sb[:, :], shared).then_inc(shared_in, 16)
            act.wait_ge(route, 2)
            act.activation(expd[:, :], top[:, :], ACT.Exp, bias=neg_max[:, 0:1], accum_out=expsum[:, 0:1])\
               .then_inc(exp_done, 1)
            act.preload_act_table(ACT.Silu)
            for n in range(E // 2 + G):
                act.wait_ge(prep_mm, n + 1)
                if n < G:
                    dst = lora_raw[:, n * GB:(n + 1) * GB, :].rearrange("p b o -> p (b o)")
                else:
                    k = 2 * (n - G)
                    dst = mix_raw[:, k:k + 2, :, :].rearrange("p k b j -> p (k b j)")
                act.activation(dst, prep[n % 2][:, :], ACT.Copy).then_inc(prep_copied, 1)

            with act.Fori(0, STEPS0) as s:
                for j in range(SLOTS0):
                    act.wait_ge(inner_done, s * SLOTS0 + (j + 1))
                    for c in range(C0):
                        act.activation(act0[:, j % FREE, c, :], pair[j % FREE][0][:, c * P:(c + 1) * P],
                                       ACT.Silu, bias=ring0[:, j, BUP0 + c:BUP0 + c + 1]).then_inc(act_done, 1)
            act.preload_act_table(ACT.Gelu_apprx_tanh)
            for g in range(G):
                act.wait_ge(lin_read, G + g + 1)
                act.activation(x_hi[:, group(g)], x[:, group(g)], ACT.Copy).then_inc(x_hi_done, 1)
            with act.Fori(0, G) as g:
                for u in range(UNITS):
                    act.wait_ge(inner_done, g * UNITS + (B + u + 1))
                    act.activation(act3[:, u % PAIRS, :], pair[u % PAIRS][0][:, :], ACT.Gelu_apprx_tanh)\
                       .then_inc(act_done, 1)

        @block.tensor
        def _(pe):
            def warm(times):
                for _ in range(times):
                    pe.matmul(acc[0][:, :], zeros[:, 0:P], zeros[:, :], start=True, stop=True)

            pe.wait_ge(zeros_set, 1)
            warm(6)
            pe.wait_ge(ones_set, 1)
            pe.wait_ge(at_diag_done, 1)
            pe.matmul(acc[1][:, 0:K * B], ones[:, :], at_diag[:, :, :].rearrange("b k n -> b (k n)"),
                      start=True, stop=True).then_inc(at_mm, 1)
            warm(3)
            for q in range(G):
                pe.wait_ge(bsw_done, q + 1)
                if q >= 2:
                    pe.wait_ge(prep_copied, q - 1)
                pe.matmul(prep[q % 2][:, :], lora_sb[:, AS1:AS1 + P],
                          bs_w[:, q * GB:(q + 1) * GB, :].rearrange("p b o -> p (b o)"),
                          start=True, stop=True).then_inc(prep_mm, 1)
            pe.wait_ge(ydelta_done, 1)
            pe.wait_ge(w2_in, 16)
            for k in range(E):
                if k == E // 2:
                    pe.wait_ge(at_done, 1)
                    pe.wait_ge(pw_diag_done, 1)
                    pe.matmul(acc[1][:, 0:K * B], ones[:, :], pw_diag[:, :, :].rearrange("b k n -> b (k n)"),
                              start=True, stop=True).then_inc(pw_mm, 1)
                n = G + k // 2
                if k % 2 == 0:
                    pe.wait_ge(prep_copied, n - 1)
                ins = pe.matmul(prep[n % 2][:, (k % 2) * B * R:(k % 2 + 1) * B * R], w2_sb[:, k, :],
                                y_delta[:, :, :].rearrange("p b j -> p (b j)"), start=True, stop=True)
                if k % 2 == 1:
                    ins.then_inc(prep_mm, 1)

            def upgate0(s, j):
                pe.wait_ge(e0_in[j], s * 16 + 16)
                pe.wait_ge(hid_done, s * (SLOTS0 * C0) + (j + 1) * C0)
                for half, (base, done) in enumerate(((UP0, inner_done), (GATE0, outer_done))):
                    for c in range(C0):
                        ins = pe.matmul(pair[j % FREE][half][:, c * P:(c + 1) * P],
                                        ring0[:, j, base + c * P:base + (c + 1) * P],
                                        x[:, cols(s * SLOTS0 + j)], start=True, stop=True)
                    ins.then_inc(done, 1)

            def down0(s, j):
                for c in range(C0):
                    pe.wait_ge(hid_done, s * (SLOTS0 * C0) + ((FREE + j) * C0 + c + 1))
                    ins = pe.matmul(acc[j % 2][:, 0:P], ring0[:, j, DOWN0 + c * P:DOWN0 + (c + 1) * P],
                                    hid0[:, j % FREE, c, :], start=(c == 0), stop=(c == C0 - 1))
                ins.then_inc(down0_done, 1)

            pe.wait_ge(pw_done, 1)
            pe.wait_ge(x_in, 16)
            with pe.Fori(0, STEPS0) as s:
                upgate0(s, 0)
                for j in range(SLOTS0):
                    if j + 1 < SLOTS0:
                        upgate0(s, j + 1)
                    down0(s, j)

            pe.wait_ge(lin1_done, G)
            pe.wait_ge(prep_copied, E // 2 + G)
            for g in range(G):
                pe.wait_ge(x1_done, x1_value(GB * g + GB - 1))
                for j in range(GB):
                    ins = pe.matmul(lin[g][:, j * P:(j + 1) * P], lin1[:, g * GB + j, :],
                                    x[:, cols(g * GB + j)], start=True, stop=True)
                ins.then_inc(lin_mm, 1)
            pe.wait_ge(lin2_done, E)
            for g in range(G):
                pe.wait_ge(lin_read, g + 1)
                for j in range(GB):
                    ins = pe.matmul(lin[g][:, j * P:(j + 1) * P], lin2[:, g * GB + j, :],
                                    x[:, cols(g * GB + j)], start=True, stop=True)
                ins.then_inc(lin_mm, 1)

            def gateup3(g, u):
                kind, c, *k = ORDER[u]
                gate, up = pair[u % PAIRS]
                if kind == "S":
                    pe.wait_ge(x_lo_done, g + 1)
                    for bank, base, done in ((gate, GATE3, inner_done), (up, UP3, outer_done)):
                        at = slice(base + c * P, base + (c + 1) * P)
                        for n, (w, v) in enumerate(((shared_hi, x_hi), (shared_hi, x_lo), (shared_lo, x_hi))):
                            ins = pe.matmul(bank[:, :], w[:, at], v[:, group(g)], start=(n == 0), stop=(n == 2))
                        ins.then_inc(done, 1)
                else:
                    slot = c * K + k[0]
                    pe.wait_ge(e3_in[slot], g * 16 + 16)
                    for bank, base, done in ((gate, GATE3, inner_done), (up, UP3, outer_done)):
                        for m in range(C3):
                            ins = pe.matmul(bank[:, m * P:(m + 1) * P],
                                            ring3[:, slot, base + m * P:base + (m + 1) * P],
                                            x[:, cols(g * GB + c)], start=True, stop=True)
                        ins.then_inc(done, 1)

            def down3(g, u):
                kind, c, *k = ORDER[u]
                if u == 0:
                    pe.wait_ge(ymain_done, g + 1)
                if u == LAST:
                    pe.wait_ge(ylast_done, g + 1)
                pe.wait_ge(hid_done, g * UNITS + (HID3 + u + 1))
                if kind == "S":
                    at = slice(DOWN3 + c * P, DOWN3 + (c + 1) * P)
                    for n, (w, v) in enumerate(((shared_hi, hid_hi), (shared_hi, hid_lo), (shared_lo, hid_hi))):
                        ins = pe.matmul(acc[0][:, :], w[:, at], v[:, :], start=(u == 0 and n == 0),
                                        stop=(u == MAIN and n == 2), skip_group_check=True)
                else:
                    y = acc[1][:, 0:P] if c == GB - 1 else acc[0][:, c * P:(c + 1) * P]
                    for m in range(C3):
                        ins = pe.matmul(y, ring3[:, c * K + k[0], DOWN3 + m * P:DOWN3 + (m + 1) * P],
                                        hid3[:, u % PAIRS, m * P:(m + 1) * P], start=(u == LAST and m == 0),
                                        stop=(u == UNITS - 1 and m == C3 - 1), skip_group_check=True)
                ins.then_inc(down3_done, 1)

            def layer3(g, last):
                for u in range(UNITS):
                    ahead = u + AHEAD
                    if ahead < UNITS or not last:
                        pe.wait_ge(hid_done, g * UNITS + (HID3 + ahead - PAIRS + 1))
                        gateup3(g + ahead // UNITS, ahead % UNITS)
                    down3(g, u)

            pe.wait_ge(hid_done, HID3)
            pe.wait_ge(x1_done, x1_value(B - 1))
            pe.wait_ge(shared_done, 1)
            gateup3(0, 0)
            pe.wait_ge(lin_read, G + 2)
            gateup3(0, 1)
            pe.wait_ge(lin_read, 2 * G)
            with pe.Fori(0, G - 1) as g:
                layer3(g, False)
            layer3(G - 1, True)

        @block.vector
        def _(dve):
            eye = cond_sb[:, E:E + B]

            dve.memset(probs[:, :], 0.0).then_inc(x1_done, SLOTS0)
            dve.memset(inv[:, :], 0.0).then_inc(hid_done, FREE * C0)
            dve.memset(expd[:, :], 0.0).then_inc(ymain_done, 1)
            dve.memset(pair_sum[:, :], 0.0).then_inc(ylast_done, 1)
            dve.wait_ge(cond_in, 16)
            dve.max(top[:, :], cond_sb[:, 0:E]).then_inc(route, 1)
            dve.wait_ge(route, 1)
            dve.tensor_scalar(neg_max[:, :], top[:, 0:1], -1.0, None, ALU.mult).then_inc(route, 1)
            dve.max_index(top_at[:, :], top[:, :], cond_sb[:, 0:E]).then_inc(route, 1)
            dve.wait_ge(route, 3)

            def diagonal(dst, src):
                return dve.tensor_tensor(dst[:, :, :], src[:, 0:K].unsqueeze(2).to_broadcast([B, K, B]),
                                         eye.unsqueeze(1).to_broadcast([B, K, B]), ALU.mult)

            diagonal(at_diag, top_at).then_inc(at_diag_done, 1)
            dve.wait_ge(at_mm, 1)
            dve.tensor_copy(at_row[:, :], acc[1][0:1, 0:K * B]).then_inc(at_done, 1)

            dve.wait_ge(rep_in, 16)
            dve.wait_ge(lora_in, 16)
            for q in range(G):
                at = slice(q * GB, (q + 1) * GB)
                dve.scalar_tensor_tensor(
                    bs_w[:, at, :], lora_sb[:, BS1:BS1 + P].unsqueeze(1).to_broadcast([P, GB, P]), LORA_SCALE,
                    cond_rep[:, at].unsqueeze(2).to_broadcast([P, GB, P]), ALU.mult, ALU.mult)\
                   .then_inc(bsw_done, 1)

            dve.wait_ge(small_in, 16)
            dve.tensor_tensor(y_delta[:, :, :], cond_rep[:, :].unsqueeze(2).to_broadcast([P, B, R]),
                              small_sb[:, DELTA:DELTA + R].unsqueeze(1).to_broadcast([P, B, R]), ALU.mult)\
               .then_inc(ydelta_done, 1)
            step = [3]

            def chained(ins):
                step[0] += 1
                ins.then_inc(route, 1)
                dve.wait_ge(route, step[0])

            dve.wait_ge(exp_done, 1)
            chained(dve.reciprocal(inv[:, 0:1], expsum[:, :]))
            chained(dve.tensor_scalar(probs[:, :], expd[:, 0:K], inv[:, 0:1], None, ALU.mult))
            chained(dve.tensor_tensor(pair_sum[:, :], probs[:, 0:1], probs[:, 1:2], ALU.add))
            chained(dve.reciprocal(inv[:, 1:2], pair_sum[:, :]))
            chained(dve.tensor_scalar(pw[:, :], probs[:, :], inv[:, 1:2], None, ALU.mult))
            chained(dve.tensor_scalar(pw_rest[:, :], pw[:, :], 1.0 - W_SCALE, None, ALU.mult))
            chained(dve.scalar_tensor_tensor(pw_all[:, :], pw[:, :], W_SCALE, pw_rest[:, :], ALU.mult, ALU.add))
            diagonal(pw_diag, pw_all).then_inc(pw_diag_done, 1)
            dve.wait_ge(pw_mm, 1)
            dve.tensor_copy(w_col[:, :], acc[1][:, 0:K * B]).then_inc(pw_done, 1)

            dve.wait_ge(x_in, 16)

            def hidden0(s, j):
                dve.wait_ge(outer_done, s * SLOTS0 + (j + 1))
                for c in range(C0):
                    dve.wait_ge(act_done, s * (SLOTS0 * C0) + (j * C0 + c + 1))
                    dve.scalar_tensor_tensor(
                        hid0[:, j % FREE, c, :], pair[j % FREE][1][:, c * P:(c + 1) * P],
                        ring0[:, j, BGATE0 + c:BGATE0 + c + 1], act0[:, j % FREE, c, :], ALU.add, ALU.mult)\
                       .then_inc(hid_done, 1)

            def result0(s, j):
                dve.wait_ge(down0_done, s * SLOTS0 + (j + 1))
                dve.scalar_tensor_tensor(x[:, cols(s * SLOTS0 + j)], acc[j % 2][:, 0:P],
                                         ring0[:, j, BDOWN0:BDOWN0 + 1], x[:, cols(s * SLOTS0 + j)],
                                         ALU.add, ALU.add).then_inc(x1_done, 1)

            with dve.Fori(0, STEPS0) as s:
                hidden0(s, 0)
                for j in range(SLOTS0):
                    if j + 1 < SLOTS0:
                        hidden0(s, j + 1)
                    result0(s, j)

            def linear(n, g):
                dve.wait_ge(lin_mm, n + 1)
                bias = small_sb[:, BIAS1:BIAS1 + 1] if n < G else small_sb[:, BIAS2:BIAS2 + 1]
                dve.scalar_tensor_tensor(x[:, group(g)], lin[g][:, :], bias, x[:, group(g)],
                                         ALU.add, ALU.add).then_inc(lin_read, 1)

            def low_part(g):
                dve.wait_ge(x_hi_done, g + 1)
                dve.tensor_tensor(x_lo[:, group(g)], x[:, group(g)], x_hi[:, group(g)].bitcast(F32),
                                  ALU.subtract).then_inc(x_lo_done, 1)

            dve.wait_ge(x1_done, x1_value(B - 1))
            for g in range(G):
                linear(g, g)
            dve.wait_ge(lin_read, G)
            for g in range(G):
                linear(G + g, g)
                if g:
                    low_part(g - 1)
            low_part(G - 1)

            def hidden(g, u):
                kind, c, *k = ORDER[u]
                s = u % PAIRS
                dve.wait_ge(act_done, g * UNITS + (ACT3 + u + 1))
                dve.wait_ge(outer_done, g * UNITS + (B + u + 1))
                if kind == "R":
                    dve.scalar_tensor_tensor(hid3[:, s, :], pair[s][1][:, :],
                                             w_col[:, bass.ds(g * GB + (k[0] * B + c), 1)], act3[:, s, :],
                                             ALU.mult, ALU.mult).then_inc(hid_done, 1)
                    return
                dve.tensor_tensor(hid3[:, s, :], pair[s][1][:, :], act3[:, s, :], ALU.mult).then_inc(split, 1)
                dve.wait_ge(split, g * (2 * GB) + (2 * c + 1))
                dve.tensor_copy(hid_hi[:, :], hid3[:, s, :]).then_inc(split, 1)
                dve.wait_ge(split, g * (2 * GB) + (2 * c + 2))
                dve.tensor_tensor(hid_lo[:, :], hid3[:, s, :], hid_hi[:, :].bitcast(F32), ALU.subtract)\
                   .then_inc(hid_done, 1)

            def result_main(g):
                dve.wait_ge(down3_done, g * UNITS + (MAIN + 1))
                dve.tensor_tensor(x[:, group(g)], acc[0][:, :], x[:, group(g)], ALU.add).then_inc(ymain_done, 1)

            def result_last(g):
                dve.wait_ge(down3_done, g * UNITS + UNITS)
                dve.wait_ge(ymain_done, g + 2)
                at = cols(g * GB + (GB - 1))
                dve.tensor_tensor(x[:, at], acc[1][:, 0:P], x[:, at], ALU.add).then_inc(ylast_done, 1)

            for u in range(UNITS):
                hidden(0, u)
            result_main(0)
            with dve.Fori(1, G) as g:
                for u in range(UNITS):
                    if u == AHEAD:
                        result_last(g - 1)
                    hidden(g, u)
                result_main(g)
            result_last(G - 1)


def kernel(x, cond_8, L0_cond_W_up, L0_cond_b_up, L0_cond_W_gate, L0_cond_b_gate, L0_cond_W_down, L0_cond_b_down,
           L1_cond_W_base, L1_cond_b_base, L1_cond_As, L1_cond_Bs, L2_cond_weight, L2_cond_mask, L2_cond_bias,
           L3_cond_skill_gate, L3_cond_skill_up, L3_cond_skill_down, L3_cond_shared_gate, L3_cond_shared_up,
           L3_cond_shared_down):
    import numpy as np
    import concourse.bacc as bacc
    from concourse.bass_utils import run_bass_kernel_spmd

    def arr(a):
        return np.asarray(a)

    def experts(parts):
        return np.ascontiguousarray(np.concatenate(parts, axis=-1))

    def down_rows(w, chunks):
        lead = w.shape[:-2]
        n = len(lead)
        w = w.reshape(*lead, chunks, P, P)
        return w.transpose(*range(n), n + 1, n, n + 2).reshape(*lead, P, chunks * P)

    def bias_cols(b, chunks):
        return arr(b).reshape(E, chunks, P).transpose(0, 2, 1)

    arrays = {
        "xT": np.ascontiguousarray(arr(x).transpose(2, 0, 1).reshape(P, B * P)),
        "cond": experts([arr(cond_8), np.eye(B, dtype=np.float32)]),
        "condT": np.ascontiguousarray(arr(cond_8).T),
        "lora": experts([arr(L1_cond_Bs).transpose(0, 2, 1).reshape(E * R, P), arr(L1_cond_As).reshape(E * R, P)]),
        "small": experts([
            arr(L1_cond_W_base).T,
            arr(L2_cond_mask).T,
            np.tile(np.eye(R, dtype=np.float32), (E, 1)),
            arr(L1_cond_b_base).reshape(P, 1),
            arr(L2_cond_bias).reshape(P, 1),
        ]),
        "w2": np.ascontiguousarray(
            arr(L2_cond_weight).reshape(E, P // R, R, P).transpose(0, 2, 1, 3).reshape(E * R, P // R, P)),
        "experts0": experts([
            arr(L0_cond_W_up).transpose(0, 2, 1),
            arr(L0_cond_W_gate).transpose(0, 2, 1),
            down_rows(arr(L0_cond_W_down).transpose(0, 2, 1), C0),
            bias_cols(L0_cond_b_up, C0),
            bias_cols(L0_cond_b_gate, C0),
            bias_cols(L0_cond_b_down, 1),
        ]),
        "experts3": experts([arr(L3_cond_skill_gate), arr(L3_cond_skill_up), down_rows(arr(L3_cond_skill_down), C3)]),
        "shared": experts([arr(L3_cond_shared_gate), arr(L3_cond_shared_up), down_rows(arr(L3_cond_shared_down), C3)]),
    }
    nc = bacc.Bacc("TRN2", target_bir_lowering=False, num_devices=1)
    args = [nc.dram_tensor(n, a.shape, mybir.dt.from_np(a.dtype), kind="ExternalInput").ap()
            for n, a in arrays.items()]
    args.append(nc.dram_tensor("out", (P, B * P), F32, kind="ExternalOutput").ap())
    build_kernel(nc, *args)
    r = run_bass_kernel_spmd(nc, [arrays], core_ids=[0])
    return r.results[0]["out"].reshape(P, B, P).transpose(1, 2, 0)
```
